# Optimizing a Trainium2 kernel written in Bass

```python
import numpy as np
import jax
import jax.numpy as jnp

def _softmax(x, axis=-1):
    return jax.nn.softmax(x, axis=axis)
def _gelu(x):
    return jax.nn.gelu(x, approximate=True)
def _silu(x):
    return jax.nn.silu(x)
def _sigmoid(x):
    return jax.nn.sigmoid(x)
def _layernorm(x, axis=-1, eps=1e-5):
    m = jnp.mean(x, axis=axis, keepdims=True)
    v = jnp.var(x, axis=axis, keepdims=True)
    return (x - m) / jnp.sqrt(v + eps)
def _scatter_add(tgt, idx, src, axis=0):
    return tgt.at[idx].add(src)
def _segment_sum(src, seg, n):
    return jax.ops.segment_sum(src, seg, n)

kernel_name = 'mk_conv_preact_d1_conv_nchw128_1e71f8'

def setup_inputs(seed: int = 0):
    np.random.seed(seed)
    _w = jnp.asarray
    def _rec_inputs():
        import jax
        import jax.numpy as jnp
        _gk = jax.random.key(seed)
        x = -0.0002023 + 1 * jax.random.normal(jax.random.fold_in(_gk, 1), (1, 128, 224, 224), jnp.float32)
        return x
    x = _rec_inputs()
    def _L0_conv_setup():
        import jax, jax.numpy as jnp
        import numpy as np
        NUM_HEAD = 4
        PATCH = (7, 7)
        GRID = (7, 7)

        def rel_pos_index(wh, ww):
            coords = np.stack(np.meshgrid(np.arange(wh), np.arange(ww), indexing='ij'))
            flat = coords.reshape(2, -1)
            rel = flat[:, :, None] - flat[:, None, :]
            rel = np.transpose(rel, (1, 2, 0)).astype(np.int64)
            rel[..., 0] += wh - 1
            rel[..., 1] += ww - 1
            rel[..., 0] *= 2 * ww - 1
            return jnp.asarray(rel.sum(-1))

        def window_partition(x, wh, ww):
            B, C, H, W = x.shape
            x = x.reshape(B, C, H // wh, wh, W // ww, ww).transpose(0, 2, 4, 3, 5, 1)
            return x.reshape(-1, wh, ww, C)

        def unbind_win(x, wh, ww, H, W):
            C = x.shape[-1]
            x = x.reshape(-1, H // wh, W // ww, wh, ww, C).transpose(0, 5, 1, 3, 4, 2)
            return x.reshape(-1, H, W, C)

        def layernorm(x, g, b, eps=1e-05):
            mu = x.mean(-1, keepdims=True)
            var = ((x - mu) ** 2).mean(-1, keepdims=True)
            return (x - mu) * jax.lax.rsqrt(var + eps) * g + b

        def mha(x, qkv_w, proj_w, proj_b, rel_table, rel_idx):
            B, N, D = x.shape
            hd = D // NUM_HEAD
            qkv = (x @ qkv_w.T).reshape(B, N, 3, NUM_HEAD, hd).transpose(2, 0, 3, 1, 4)
            q, k, v = (qkv[0], qkv[1], qkv[2])
            attn = jnp.einsum('bhnd,bhmd->bhnm', q, k) * hd ** 0.5
            bias = rel_table[rel_idx.reshape(-1)].reshape(N, N, NUM_HEAD).transpose(2, 0, 1)
            attn = jax.nn.softmax(attn + bias[None], axis=-1)
            out = jnp.einsum('bhnm,bhmd->bhnd', attn, v).transpose(0, 2, 1, 3).reshape(B, N, D)
            return out @ proj_w.T + proj_b

        def tblock(x, rel_table, rel_idx, qkv_w, proj_w, proj_b, ln_g, ln_b, fc1_w, fc1_b, fc2_w, fc2_b):
            net = mha(x, qkv_w, proj_w, proj_b, rel_table, rel_idx) + x
            net = layernorm(net, ln_g, ln_b)
            shortcut = net
            net = net @ fc1_w.T + fc1_b
            net = net @ fc2_w.T + fc2_b
            return net + shortcut

        def _forward(x, b_rel_table, b_qkv_w, b_proj_w, b_proj_b, b_ln_g, b_ln_b, b_fc1_w, b_fc1_b, b_fc2_w, b_fc2_b, g_rel_table, g_qkv_w, g_proj_w, g_proj_b, g_ln_g, g_ln_b, g_fc1_w, g_fc1_b, g_fc2_w, g_fc2_b):
            H, W = (x.shape[2], x.shape[3])
            ph, pw = PATCH
            gh, gw = (H // GRID[0], W // GRID[1])
            idx_b = rel_pos_index(ph, pw)
            idx_g = rel_pos_index(gh, gw)
            net = window_partition(x, ph, pw)
            nb, h, w, ch = net.shape
            net = tblock(net.reshape(nb, h * w, ch), b_rel_table, idx_b, b_qkv_w, b_proj_w, b_proj_b, b_ln_g, b_ln_b, b_fc1_w, b_fc1_b, b_fc2_w, b_fc2_b)
            net = unbind_win(net.reshape(nb, h, w, ch), ph, pw, H, W).transpose(0, 3, 1, 2)
            net = window_partition(net, gh, gw)
            nb, h, w, ch = net.shape
            net = tblock(net.reshape(nb, h * w, ch), g_rel_table, idx_g, g_qkv_w, g_proj_w, g_proj_b, g_ln_g, g_ln_b, g_fc1_w, g_fc1_b, g_fc2_w, g_fc2_b)
            net = unbind_win(net.reshape(nb, h, w, ch), gh, gw, H, W).transpose(0, 3, 1, 2)
            return net
        key = jax.random.key(seed)
        ks = jax.random.split(key, 24)
        C, E = (128, 512)

        def rn(k, shape, s=0.05):
            return jax.random.normal(k, shape, dtype=jnp.float32) * s
        inp = {'x': rn(ks[0], (1, C, 224, 224), 1.0)}
        for i, p in enumerate(['b', 'g']):
            tbl = (2 * 7 - 1) ** 2 if p == 'b' else (2 * 32 - 1) ** 2
            o = i * 5
            inp[p + '_rel_table'] = rn(ks[1 + o], (tbl, NUM_HEAD), 0.02)
            inp[p + '_qkv_w'] = rn(ks[2 + o], (3 * C, C))
            inp[p + '_proj_w'] = rn(ks[3 + o], (C, C))
            inp[p + '_proj_b'] = jnp.zeros((C,), jnp.float32)
            inp[p + '_ln_g'] = jnp.ones((C,), jnp.float32)
            inp[p + '_ln_b'] = jnp.zeros((C,), jnp.float32)
            inp[p + '_fc1_w'] = rn(ks[4 + o], (E, C))
            inp[p + '_fc1_b'] = jnp.zeros((E,), jnp.float32)
            inp[p + '_fc2_w'] = rn(ks[5 + o], (C, E))
            inp[p + '_fc2_b'] = jnp.zeros((C,), jnp.float32)
        return inp
    _L0_conv_all = _L0_conv_setup()
    _L0_conv_in = {k: v for k, v in _L0_conv_all.items() if k in ('b_rel_table', 'b_qkv_w', 'b_proj_w', 'b_proj_b', 'b_ln_g', 'b_ln_b', 'b_fc1_w', 'b_fc1_b', 'b_fc2_w', 'b_fc2_b', 'g_rel_table', 'g_qkv_w', 'g_proj_w', 'g_proj_b', 'g_ln_g', 'g_ln_b', 'g_fc1_w', 'g_fc1_b', 'g_fc2_w', 'g_fc2_b', )}
    del _L0_conv_all

    return {
        "x": x,
        "L0_conv_b_rel_table": _L0_conv_in["b_rel_table"],
        "L0_conv_b_qkv_w": _L0_conv_in["b_qkv_w"],
        "L0_conv_b_proj_w": _L0_conv_in["b_proj_w"],
        "L0_conv_b_proj_b": _L0_conv_in["b_proj_b"],
        "L0_conv_b_ln_g": _L0_conv_in["b_ln_g"],
        "L0_conv_b_ln_b": _L0_conv_in["b_ln_b"],
        "L0_conv_b_fc1_w": _L0_conv_in["b_fc1_w"],
        "L0_conv_b_fc1_b": _L0_conv_in["b_fc1_b"],
        "L0_conv_b_fc2_w": _L0_conv_in["b_fc2_w"],
        "L0_conv_b_fc2_b": _L0_conv_in["b_fc2_b"],
        "L0_conv_g_rel_table": _L0_conv_in["g_rel_table"],
        "L0_conv_g_qkv_w": _L0_conv_in["g_qkv_w"],
        "L0_conv_g_proj_w": _L0_conv_in["g_proj_w"],
        "L0_conv_g_proj_b": _L0_conv_in["g_proj_b"],
        "L0_conv_g_ln_g": _L0_conv_in["g_ln_g"],
        "L0_conv_g_ln_b": _L0_conv_in["g_ln_b"],
        "L0_conv_g_fc1_w": _L0_conv_in["g_fc1_w"],
        "L0_conv_g_fc1_b": _L0_conv_in["g_fc1_b"],
        "L0_conv_g_fc2_w": _L0_conv_in["g_fc2_w"],
        "L0_conv_g_fc2_b": _L0_conv_in["g_fc2_b"],
    }

def reference(x, L0_conv_b_rel_table, L0_conv_b_qkv_w, L0_conv_b_proj_w, L0_conv_b_proj_b, L0_conv_b_ln_g, L0_conv_b_ln_b, L0_conv_b_fc1_w, L0_conv_b_fc1_b, L0_conv_b_fc2_w, L0_conv_b_fc2_b, L0_conv_g_rel_table, L0_conv_g_qkv_w, L0_conv_g_proj_w, L0_conv_g_proj_b, L0_conv_g_ln_g, L0_conv_g_ln_b, L0_conv_g_fc1_w, L0_conv_g_fc1_b, L0_conv_g_fc2_w, L0_conv_g_fc2_b):
    import jax
    import jax.numpy as jnp
    def _L0_conv_ref(x, b_rel_table, b_qkv_w, b_proj_w, b_proj_b, b_ln_g, b_ln_b, b_fc1_w, b_fc1_b, b_fc2_w, b_fc2_b, g_rel_table, g_qkv_w, g_proj_w, g_proj_b, g_ln_g, g_ln_b, g_fc1_w, g_fc1_b, g_fc2_w, g_fc2_b):
        import jax, jax.numpy as jnp
        import numpy as np
        NUM_HEAD = 4
        PATCH = (7, 7)
        GRID = (7, 7)

        def rel_pos_index(wh, ww):
            coords = np.stack(np.meshgrid(np.arange(wh), np.arange(ww), indexing='ij'))
            flat = coords.reshape(2, -1)
            rel = flat[:, :, None] - flat[:, None, :]
            rel = np.transpose(rel, (1, 2, 0)).astype(np.int64)
            rel[..., 0] += wh - 1
            rel[..., 1] += ww - 1
            rel[..., 0] *= 2 * ww - 1
            return jnp.asarray(rel.sum(-1))

        def window_partition(x, wh, ww):
            B, C, H, W = x.shape
            x = x.reshape(B, C, H // wh, wh, W // ww, ww).transpose(0, 2, 4, 3, 5, 1)
            return x.reshape(-1, wh, ww, C)

        def unbind_win(x, wh, ww, H, W):
            C = x.shape[-1]
            x = x.reshape(-1, H // wh, W // ww, wh, ww, C).transpose(0, 5, 1, 3, 4, 2)
            return x.reshape(-1, H, W, C)

        def layernorm(x, g, b, eps=1e-05):
            mu = x.mean(-1, keepdims=True)
            var = ((x - mu) ** 2).mean(-1, keepdims=True)
            return (x - mu) * jax.lax.rsqrt(var + eps) * g + b

        def mha(x, qkv_w, proj_w, proj_b, rel_table, rel_idx):
            B, N, D = x.shape
            hd = D // NUM_HEAD
            qkv = (x @ qkv_w.T).reshape(B, N, 3, NUM_HEAD, hd).transpose(2, 0, 3, 1, 4)
            q, k, v = (qkv[0], qkv[1], qkv[2])
            attn = jnp.einsum('bhnd,bhmd->bhnm', q, k) * hd ** 0.5
            bias = rel_table[rel_idx.reshape(-1)].reshape(N, N, NUM_HEAD).transpose(2, 0, 1)
            attn = jax.nn.softmax(attn + bias[None], axis=-1)
            out = jnp.einsum('bhnm,bhmd->bhnd', attn, v).transpose(0, 2, 1, 3).reshape(B, N, D)
            return out @ proj_w.T + proj_b

        def tblock(x, rel_table, rel_idx, qkv_w, proj_w, proj_b, ln_g, ln_b, fc1_w, fc1_b, fc2_w, fc2_b):
            net = mha(x, qkv_w, proj_w, proj_b, rel_table, rel_idx) + x
            net = layernorm(net, ln_g, ln_b)
            shortcut = net
            net = net @ fc1_w.T + fc1_b
            net = net @ fc2_w.T + fc2_b
            return net + shortcut

        def _forward(x, b_rel_table, b_qkv_w, b_proj_w, b_proj_b, b_ln_g, b_ln_b, b_fc1_w, b_fc1_b, b_fc2_w, b_fc2_b, g_rel_table, g_qkv_w, g_proj_w, g_proj_b, g_ln_g, g_ln_b, g_fc1_w, g_fc1_b, g_fc2_w, g_fc2_b):
            H, W = (x.shape[2], x.shape[3])
            ph, pw = PATCH
            gh, gw = (H // GRID[0], W // GRID[1])
            idx_b = rel_pos_index(ph, pw)
            idx_g = rel_pos_index(gh, gw)
            net = window_partition(x, ph, pw)
            nb, h, w, ch = net.shape
            net = tblock(net.reshape(nb, h * w, ch), b_rel_table, idx_b, b_qkv_w, b_proj_w, b_proj_b, b_ln_g, b_ln_b, b_fc1_w, b_fc1_b, b_fc2_w, b_fc2_b)
            net = unbind_win(net.reshape(nb, h, w, ch), ph, pw, H, W).transpose(0, 3, 1, 2)
            net = window_partition(net, gh, gw)
            nb, h, w, ch = net.shape
            net = tblock(net.reshape(nb, h * w, ch), g_rel_table, idx_g, g_qkv_w, g_proj_w, g_proj_b, g_ln_g, g_ln_b, g_fc1_w, g_fc1_b, g_fc2_w, g_fc2_b)
            net = unbind_win(net.reshape(nb, h, w, ch), gh, gw, H, W).transpose(0, 3, 1, 2)
            return net
        return _forward(x, b_rel_table, b_qkv_w, b_proj_w, b_proj_b, b_ln_g, b_ln_b, b_fc1_w, b_fc1_b, b_fc2_w, b_fc2_b, g_rel_table, g_qkv_w, g_proj_w, g_proj_b, g_ln_g, g_ln_b, g_fc1_w, g_fc1_b, g_fc2_w, g_fc2_b)

    def _gn(v, G=32, eps=1e-5):
        B_, C_, H_, W_ = v.shape
        g = v.reshape(B_, G, C_ // G, H_, W_)
        m = jnp.mean(g, axis=(2, 3, 4), keepdims=True)
        s = jnp.var(g, axis=(2, 3, 4), keepdims=True)
        return ((g - m) / jnp.sqrt(s + eps)).reshape(v.shape)

    def _ln_c(v, eps=1e-6):
        m = jnp.mean(v, axis=1, keepdims=True)
        s = jnp.var(v, axis=1, keepdims=True)
        return (v - m) / jnp.sqrt(s + eps)

    def _ln_t(v, eps=1e-5):
        m = jnp.mean(v, axis=-1, keepdims=True)
        s = jnp.var(v, axis=-1, keepdims=True)
        return (v - m) / jnp.sqrt(s + eps)

    def _to_tokens(v):
        B_, C_, H_, W_ = v.shape
        return v.reshape(B_, C_, H_ * W_).transpose(0, 2, 1)
    def _from_tokens(t, like):
        B_, C_, H_, W_ = like.shape
        return t.transpose(0, 2, 1).reshape(B_, C_, H_, W_)

    x = x + _L0_conv_ref(_gn(x), L0_conv_b_rel_table, L0_conv_b_qkv_w, L0_conv_b_proj_w, L0_conv_b_proj_b, L0_conv_b_ln_g, L0_conv_b_ln_b, L0_conv_b_fc1_w, L0_conv_b_fc1_b, L0_conv_b_fc2_w, L0_conv_b_fc2_b, L0_conv_g_rel_table, L0_conv_g_qkv_w, L0_conv_g_proj_w, L0_conv_g_proj_b, L0_conv_g_ln_g, L0_conv_g_ln_b, L0_conv_g_fc1_w, L0_conv_g_fc1_b, L0_conv_g_fc2_w, L0_conv_g_fc2_b)
    return x


_drawn_inputs = setup_inputs


def setup_inputs(seed=0):
    import zlib

    import numpy as np

    out = dict(_drawn_inputs(seed))
    spreads = {'L0_conv_b_proj_b': (0.0, 0.1),
     'L0_conv_b_ln_g': (1.0, 0.2),
     'L0_conv_b_ln_b': (0.0, 0.1),
     'L0_conv_b_fc1_b': (0.0, 0.1),
     'L0_conv_b_fc2_b': (0.0, 0.1),
     'L0_conv_g_proj_b': (0.0, 0.1),
     'L0_conv_g_ln_g': (1.0, 0.2),
     'L0_conv_g_ln_b': (0.0, 0.1),
     'L0_conv_g_fc1_b': (0.0, 0.1),
     'L0_conv_g_fc2_b': (0.0, 0.1)}
    factors = {'L0_conv_b_rel_table': 21.738, 'L0_conv_g_rel_table': 45.719}
    for name, (base, spread) in spreads.items():
        noise = np.random.default_rng([zlib.crc32(name.encode()), seed]).standard_normal(out[name].shape)
        drawn = base * np.exp(spread * noise) if base else spread * noise
        out[name] = jnp.asarray(drawn.astype(out[name].dtype))
    for name, factor in factors.items():
        out[name] = (out[name] * factor).astype(out[name].dtype)
    return out
```

```python
from contextlib import ExitStack

import numpy as np

import concourse.bass as bass
from concourse import mybir

F32 = mybir.dt.float32
F16 = mybir.dt.float16
ALU = mybir.AluOpType
ACT = mybir.ActivationFunctionType
AX_X = mybir.AxisListType.X

P = 128
NH, HD = 4, 32
HW = 224
E = 512
ET = E // P
EPS = 1e-5
SCALE = float(HD) ** 0.5

BW = 7
BT = BW * BW
STRIP = BW * HW
NSTRIP = HW // BW
WPS = HW // BW
UPS = 4
WPU = WPS // UPS
PPU = WPU // 2
UT = WPU * BT
PAD = 64
BREL = 2 * BW - 1

GW = 32
GT = GW * GW
GN_ = HW // GW
NWIN = GN_ * GN_
QT = GT // P
UNITS = QT * NH
HALF = GT // 2
GREL = 2 * GW - 1
TPP = GT // P
RPT = P // GW
GSPAN = GW + (QT - 1) * RPT
QG = 2
GROUP = QG * NH
LAG = GROUP + 2

STAT_COLS = 512
STAT_PER = 2
CHUNKS_IN = 7
CHUNK = STAT_COLS * STAT_PER
NCHUNK = HW * HW // CHUNK


def there(v, n):
    return not isinstance(v, int) or 0 <= v < n


def positive(v):
    return not isinstance(v, int) or v > 0


def spread(ap, dim, n):
    dims = [list(d) for d in ap.ap]
    dims.insert(dim, [0, n])
    return bass.AP(ap.tensor, ap.offset, dims)


KINDS = ("w", "var", "y", "k", "q", "r", "pj", "cz", "v", "o", "t")
GRID_TURNS = [("var", 0, -1, 0), ("y", 0, -1, 0), ("w", 0, 1, 0), ("w", 1, 1, 0), ("k", 0, 1, 0),
              ("k", 1, 1, 0), ("r", 1, -1, 0), ("pj", 1, -1, 0), ("cz", 1, -1, 0), ("q", 0, 1, 0),
              ("var", 1, -1, 0), ("y", 1, -1, 0), ("q", 1, 1, 0), ("v", 0, 1, 0), ("v", 1, 1, 0),
              ("r", 0, 0, 0), ("pj", 0, 0, 0), ("cz", 0, 0, 0)]
TURN_STEPS = [1, 2, 3, 4, 6, 9, 10, 12, 14, 17, 18, 19, 20, 21, 24, 26, 27, 31]
BLOCK_TURNS = [("pj", 0, -2, 0), ("t", 0, -1, 2), ("t", 1, -1, 3), ("cz", 0, -2, 1), ("v", 0, UPS, 0),
               ("var", 0, -2, 1), ("o", 0, -1, 2), ("y", 0, -2, 3), ("q", 0, UPS, 0), ("k", 0, UPS, 1)]
GRID_PER = {kind: 2 for kind in KINDS}
BLOCK_PER = {kind: 2 if kind == "t" else 1 for kind in KINDS}


def tenant_before(turns, per, step, k, n):
    bank = turns[k][3]
    while True:
        k -= 1
        if k < 0:
            k += len(turns)
            step = step - 1
        kind, half, off, its_bank = turns[k]
        if its_bank != bank:
            continue
        at = step + off
        if there(at, n):
            return kind, at * per[kind] + half + 1
        if isinstance(step, int) and step < -UPS - 2:
            return None


def build(nc, x, w, out, net1, net2):
    x_flat = x.rearrange("a c h w -> (a c) (h w)")
    out_flat = out.rearrange("a c h w -> (a c) (h w)")
    net_flat = net1.rearrange("c h w -> c (h w)")

    with ExitStack() as ctx:
        def sb(name, shape, dt=F32, on=ctx):
            return on.enter_context(nc.sbuf_tensor(name, shape, dt))

        ident = sb("ident", [P, P])
        center = sb("center", [P, P])
        mean_w = sb("mean_w", [P, P])
        eps = sb("eps", [P, 1])
        gn_scale = sb("gn_scale", [P, 1])
        gn_shift = sb("gn_shift", [P, 1])
        qkv_t = {p: sb(f"qkv_t_{p}", [P, 3 * P]) for p in "bg"}
        proj_t = {p: sb(f"proj_t_{p}", [P, P]) for p in "bg"}
        mlp_t = {p: sb(f"mlp_t_{p}", [P, P]) for p in "bg"}
        proj_b = {p: sb(f"proj_b_{p}", [P, 1]) for p in "bg"}
        out_b = {p: sb(f"out_b_{p}", [P, 1]) for p in "bg"}
        gbias = sb("gbias", [P, NH, GSPAN, GW])
        bbias = sb("bbias", [P, NH, BT])

        kept = dict(ident=ident, center=center, mean_w=mean_w, eps=eps, gn_scale=gn_scale, gn_shift=gn_shift,
                    qkv_t=qkv_t, proj_t=proj_t, mlp_t=mlp_t, proj_b=proj_b, out_b=out_b,
                    gbias=gbias, bbias=bbias)
        with ExitStack() as own:
            setup_stage(nc, own, x_flat, w, kept)
        with ExitStack() as own:
            block_stage(nc, own, x_flat, net_flat, kept)
        with ExitStack() as own:
            grid_stage(nc, own, net1, net2, kept)
        with ExitStack() as own:
            last_stage(nc, own, x_flat, net2, out_flat, kept)


def setup_stage(nc, own, x_flat, w, c):
    def sb(name, shape, dt=F32):
        return own.enter_context(nc.sbuf_tensor(name, shape, dt))

    def sem(name):
        return own.enter_context(nc.semaphore(name))

    ident, center, mean_w, eps = c["ident"], c["center"], c["mean_w"], c["eps"]
    gbias, bbias = c["gbias"], c["bbias"]
    chunk = sb("chunk", [P, CHUNKS_IN, CHUNK])
    stats = sb("stats", [P, NCHUNK * STAT_PER, 6])
    mean_var = sb("mean_var", [P, 2])
    group_avg = sb("group_avg", [P, P])
    small = sb("small", [P, 8])
    gbias_in = sb("gbias_in", [GW, NH, GREL, GW])
    bbias_in = sb("bbias_in", [P, NH, BT])
    flip_g, flip_b = sb("flip_g", [GW, GW]), sb("flip_b", [P, P])
    fc1 = {p: sb(f"fc1_{p}", [P, ET, P]) for p in "bg"}
    fc2_t = {p: sb(f"fc2_t_{p}", [P, ET, P]) for p in "bg"}
    vecs = {p: sb(f"vecs_{p}", [P, 3 + ET]) for p in "bg"}
    m_t = {p: sb(f"m_t_{p}", [P, P]) for p in "bg"}
    gm_t = {p: sb(f"gm_t_{p}", [P, P]) for p in "bg"}
    ps = own.enter_context(nc.psum_tensor("ps_setup", [P, 8, 512], F32))

    loaded = sem("weights_loaded")
    bias_zero = sem("bias_zero")
    bias_loaded = sem("bias_loaded")
    reordered = sem("reordered")
    bias_kept = sem("bias_kept")
    chunk_in = [sem(f"chunk_in{b}") for b in range(CHUNKS_IN)]
    chunk_used = sem("chunk_used")
    made = sem("constants_made")
    dve = sem("setup_dve")
    pe = sem("setup_pe")
    act = sem("setup_act")

    n_loads = 0
    groups = NCHUNK // CHUNKS_IN

    with nc.Block() as block:
        @block.sync
        def _(sp):
            def load_chunk(i, b):
                sp.dma_start(chunk[:, b, :], x_flat[:, bass.ds((i * CHUNKS_IN + b) * CHUNK, CHUNK)]
                             ).then_inc(chunk_in[b], 16)

            for b in range(CHUNKS_IN):
                load_chunk(0, b)
            with sp.Fori(1, groups) as i:
                for b in range(CHUNKS_IN):
                    sp.wait_ge(chunk_used, (i - 1) * CHUNKS_IN + b + 1)
                    load_chunk(i, b)

        @block.scalar
        def _(eng):
            nc.scalar.preload_act_table_set("natural_log_exp_and_others")
            n = 0
            for p in "bg":
                for dst, src in (
                    (c["qkv_t"][p][:, :], w[p + "_qkv_t"]),
                    (c["proj_t"][p][:, :], w[p + "_proj_t"]),
                    (fc1[p][:, :, :], w[p + "_fc1_w"].rearrange("(t p) c -> p t c", p=P)),
                    (fc2_t[p][:, :, :], w[p + "_fc2_t"].rearrange("(t p) c -> p t c", p=P)),
                    (c["proj_b"][p][:, :], w[p + "_proj_b"]),
                    (vecs[p][:, 0:1], w[p + "_ln_g"]),
                    (vecs[p][:, 1:2], w[p + "_ln_b"]),
                    (vecs[p][:, 2:3], w[p + "_fc2_b"]),
                    (vecs[p][:, 3:3 + ET], w[p + "_fc1_b"]),
                ):
                    eng.dma_start(dst, src).then_inc(loaded, 16)
                    n += 1
            assert n == N_LOADS
            table = w["g_table"]
            for h in range(NH):
                src = bass.AP(table.tensor, h * GREL * GREL, [[1, GW], [GREL, GREL], [1, GW]])
                eng.dma_start(gbias_in[:, h, :, :], src).then_inc(bias_loaded, 16)
            eng.wait_ge(bias_zero, 1)
            table = w["b_table"]
            for par in range(2):
                for i in range(BW):
                    for h in range(NH):
                        src = bass.AP(table.tensor, h * BREL * BREL + (BW - 1 - i) * BREL,
                                      [[1, BW], [BREL, BW], [1, BW]])
                        dst = bbias_in[PAD * par + BW * i:PAD * par + BW * (i + 1), h, :]
                        eng.dma_start(dst.rearrange("p (a b) -> p a b", a=BW), src).then_inc(bias_loaded, 16)
            for n in range(BIAS_PIECES):
                h, e = n // (GSPAN // PIECE_ROWS), n % (GSPAN // PIECE_ROWS) * PIECE_ROWS
                eng.wait_ge(reordered, n + 1)
                eng.activation(gbias[:, h, e:e + PIECE_ROWS, :], ps[:, n % 2, 0:PIECE_ROWS * GW],
                               ACT.Copy, scale=-1.0).then_inc(bias_kept, 1)
            eng.wait_ge(reordered, BIAS_PIECES + 1)
            eng.activation(bbias[:, :, :].rearrange("p h m -> p (h m)"), ps[:, BIAS_PIECES % 2, 0:NH * BT],
                           ACT.Copy).then_inc(bias_kept, 1)
            eng.wait_ge(dve, D_GROUPVAR)
            eng.activation(small[:, 4:5], small[:, 3:4], ACT.Ln, bias=eps[:, 0:1]).then_inc(act, 1)
            eng.wait_ge(act, 1)
            eng.activation(c["gn_scale"][:, :], small[:, 4:5], ACT.Exp, scale=-0.5).then_inc(act, 1)

        @block.gpsimd
        def _(pool):
            pool.memset(bbias_in[:, :, :], 0.0).then_inc(bias_zero, 1)
            pool.memset(ident[:, :], 0.0).then_inc(made, 1)
            pool.memset(group_avg[:, :], 0.25).then_inc(made, 1)
            pool.memset(mean_w[:, :], 1.0 / P).then_inc(made, 1)
            pool.memset(eps[:, :], EPS).then_inc(made, 1)
            pool.memset(flip_g[:, :], 0.0).then_inc(made, 1)
            pool.memset(flip_b[:, :], 0.0).then_inc(made, 1)
            pool.wait_ge(made, 6)
            pool.affine_select(out=ident[:, :], in_=ident[:, :], compare_op=ALU.not_equal, fill=1.0,
                               base=0, pattern=[[-1, P]], channel_multiplier=1).then_inc(made, 1)
            g3 = group_avg[:, :].rearrange("p (g k) -> p g k", k=4)
            pool.affine_select(out=g3, in_=g3, compare_op=ALU.is_ge, fill=0.0, base=0,
                               pattern=[[-4, P // 4], [0, 4]], channel_multiplier=1).then_inc(made, 1)
            pool.wait_ge(made, 8)
            pool.affine_select(out=g3, in_=g3, compare_op=ALU.is_ge, fill=0.0, base=3,
                               pattern=[[4, P // 4], [0, 4]], channel_multiplier=-1).then_inc(made, 1)
            pool.affine_select(out=flip_g[:, :], in_=flip_g[:, :], compare_op=ALU.not_equal, fill=1.0,
                               base=-(GW - 1), pattern=[[1, GW]], channel_multiplier=1).then_inc(made, 1)
            for first in FLIPS_B:
                v = flip_b[:, first:first + BW]
                pool.affine_select(out=v, in_=v, compare_op=ALU.not_equal, fill=1.0, base=-(first + BW - 1),
                                   pattern=[[1, BW]], channel_multiplier=1).then_inc(made, 1)

        @block.tensor
        def _(t):
            t.wait_ge(loaded, 16 * N_LOADS)
            for n, p in enumerate("bg"):
                for e in range(ET):
                    mm = t.matmul(ps[:, n, 0:P], fc1[p][:, e, :], fc2_t[p][:, e, :],
                                  start=(e == 0), stop=(e == ET - 1))
                mm.then_inc(pe, 1)
            for n, p in enumerate("bg"):
                t.wait_ge(dve, 1 + 3 * n + 2)
                t.matmul(ps[:, 2 + n, 0:P], center[:, :], gm_t[p][:, :], start=True, stop=True)
                t.matmul(ps[:, 4 + n, 0:1], m_t[p][:, :], vecs[p][:, 1:2], start=True, stop=False)
                for e in range(ET):
                    mm = t.matmul(ps[:, 4 + n, 0:1], fc2_t[p][:, e, :], vecs[p][:, 3 + e:4 + e],
                                  start=False, stop=(e == ET - 1))
                mm.then_inc(pe, 1)
            t.wait_ge(made, 10 + len(FLIPS_B))
            t.wait_ge(bias_loaded, 16 * NH * (1 + 2 * BW))
            for n in range(BIAS_PIECES):
                if n >= 2:
                    t.wait_ge(bias_kept, n - 1)
                h, e = n // (GSPAN // PIECE_ROWS), n % (GSPAN // PIECE_ROWS) * PIECE_ROWS
                for a in range(RPT):
                    at = e + RPT - 1 - a
                    mm = t.matmul(ps[GW * a:GW * (a + 1), n % 2, 0:PIECE_ROWS * GW], flip_g[:, :],
                                  gbias_in[:, h, at:at + PIECE_ROWS, :].rearrange("p e j -> p (e j)"),
                                  start=True, stop=True)
                mm.then_inc(reordered, 1)
            t.wait_ge(bias_kept, BIAS_PIECES - 1)
            t.matmul(ps[:, BIAS_PIECES % 2, 0:NH * BT], flip_b[:, :], bbias_in[:, :, :].rearrange("p h m -> p (h m)"),
                     start=True, stop=True).then_inc(reordered, 1)
            t.wait_ge(dve, D_STATS)
            t.matmul(ps[:, 6, 0:1], group_avg[:, :], mean_var[:, 0:1], start=True, stop=True).then_inc(pe, 1)
            t.wait_ge(dve, D_STATS + 3)
            t.matmul(ps[:, 7, 0:1], group_avg[:, :], small[:, 2:3], start=True, stop=True).then_inc(pe, 1)

        @block.vector
        def _(v):
            at = 0

            def link(ins):
                nonlocal at
                at += 1
                ins.then_inc(dve, 1)
                v.wait_ge(dve, at)

            def take_stats(first, last):
                with v.Fori(first, last) as i:
                    for b in range(CHUNKS_IN):
                        v.wait_ge(chunk_in[b], (i + 1) * 16)
                        for k in range(STAT_PER):
                            at_col = (i * CHUNKS_IN + b) * STAT_PER + k
                            ins = v.bn_stats(stats[:, bass.ds(at_col, 1), :],
                                             chunk[:, b, k * STAT_COLS:(k + 1) * STAT_COLS])
                        ins.then_inc(chunk_used, 1)

            take_stats(0, groups // 2)
            v.wait_ge(made, 9)
            v.wait_ge(loaded, 16 * N_LOADS)
            link(v.tensor_scalar(center[:, :], ident[:, :], -1.0 / P, None, ALU.add))
            for n, p in enumerate("bg"):
                v.wait_ge(pe, n + 1)
                link(v.tensor_tensor(m_t[p][:, :], ps[:, n, 0:P], ident[:, :], ALU.add))
                link(v.tensor_scalar(gm_t[p][:, :], m_t[p][:, :], vecs[p][:, 0:1], None, ALU.mult))
                sign = 1.0 if p == "b" else -1.0
                link(v.tensor_scalar(c["qkv_t"][p][:, 0:P], c["qkv_t"][p][:, 0:P], sign * SCALE, None, ALU.mult))
            for n, p in enumerate("bg"):
                v.wait_ge(pe, 2 + n + 1)
                link(v.tensor_copy(c["mlp_t"][p][:, :], ps[:, 2 + n, 0:P]))
                link(v.tensor_scalar(c["out_b"][p][:, :], ps[:, 4 + n, 0:1], vecs[p][:, 2:3], None, ALU.add))
            assert at == D_STATS - 1
            take_stats(groups // 2, groups)
            v.wait_ge(chunk_used, NCHUNK)
            link(v.bn_aggr(mean_var[:, :], stats[:, :, :].rearrange("p a b -> p (a b)")))
            v.wait_ge(pe, 5)
            link(v.tensor_tensor(small[:, 1:2], mean_var[:, 0:1], ps[:, 6, 0:1], ALU.subtract))
            link(v.tensor_tensor(small[:, 5:6], small[:, 1:2], small[:, 1:2], ALU.mult))
            link(v.tensor_tensor(small[:, 2:3], small[:, 5:6], mean_var[:, 1:2], ALU.add))
            v.wait_ge(pe, 6)
            link(v.tensor_copy(small[:, 3:4], ps[:, 7, 0:1]))
            assert at == D_GROUPVAR
            v.wait_ge(act, 2)
            link(v.tensor_tensor(small[:, 6:7], ps[:, 6, 0:1], c["gn_scale"][:, :], ALU.mult))
            link(v.tensor_scalar(c["gn_shift"][:, :], small[:, 6:7], -1.0, None, ALU.mult))


N_LOADS = 18
PIECE_ROWS = 15
BIAS_PIECES = NH * GSPAN // PIECE_ROWS
FLIPS_B = [PAD * par + BW * i for par in range(2) for i in range(BW)]
D_STATS = 1 + 2 * 3 + 2 * 2 + 1
D_GROUPVAR = D_STATS + 4


def restack(dma, stack, high, low, cols, copies, done):
    n_cols = cols.stop - cols.start
    for h in range(NH):
        for n, low_part in enumerate(copies):
            src = (low if low_part else high)[HD * h:HD * (h + 1), cols]
            dma.dma_start(stack[HD * n:HD * (n + 1), h, 0:n_cols], src).then_inc(done, 16)


Q_COPIES = (False, True, False, True)
K_COPIES = (False, False, True, True)
RESTACK = 16 * NH * 4


def block_stage(nc, own, x_flat, net_flat, c):
    def sb(name, shape, dt=F32):
        return own.enter_context(nc.sbuf_tensor(name, shape, dt))

    def sem(name):
        return own.enter_context(nc.semaphore(name))

    WIDE = STRIP + PAD - BT
    HS = STRIP // 2
    strip = sb("strip", [P, STRIP])
    xn = sb("xn", [P, 2, WIDE])
    res = sb("res", [P, 2, STRIP])
    parts = sb("parts", [P, 4, STRIP], F16)
    stack = [sb(f"stack{h}", [P, 2, NH, HS + PAD - BT], F16) for h in range(2)]
    vals = sb("vals", [P, 2, UPS, WPU * 2 * 2 * HD])
    score = sb("score", [P, NH * PPU, BT])
    shifted = sb("shifted", [P, NH * PPU, BT])
    expd = sb("expd", [P, NH * PPU, BT])
    probs = sb("probs", [P, 2, PPU, NH, PAD])
    probs_t = sb("probs_t", [P, 2, 2 * PPU, P])
    row_max = sb("row_max", [P, 2, NH * PPU])
    row_sum = sb("row_sum", [P, 2, NH * PPU])
    row_inv = sb("row_inv", [P, 2, NH * PPU])
    att = sb("att", [P, 2, UT])
    z = sb("z", [P, 2, UT])
    sq = sb("sq", [P, UT])
    lnv = sb("lnv", [P, UT])
    rstd = sb("rstd", [P, UT])
    y = sb("y", [P, 2, UT])
    done_strip = sb("done_strip", [P, 2, STRIP])
    s_ps = own.enter_context(nc.psum_tensor("s_ps", [P, 2, NH, 256], F32))
    m_ps = own.enter_context(nc.psum_tensor("m_ps", [P, 4, 512], F32))

    zeroed = sem("b_zeroed")
    x_in = sem("b_x_in")
    normed = sem("b_normed")
    res_made = sem("b_res_made")
    stacked = [sem(f"b_stacked{h}") for h in range(2)]
    scored = sem("b_scored")
    biased = sem("b_biased")
    maxed = sem("b_maxed")
    shift_done = sem("b_shift_done")
    exp_done = sem("b_exp_done")
    summed = sem("b_summed")
    inverted = sem("b_inverted")
    probs_made = sem("b_probs_made")
    high_made = {k: sem(f"b_{k}_high") for k in "qk"}
    made = {k: sem(f"b_pe_{k}") for k in KINDS}
    taken = {k: sem(f"b_took_{k}") for k in KINDS}
    lnv_made = sem("b_lnv_made")
    rstd_made = sem("b_rstd_made")
    unit_done = sem("b_unit_done")
    stored = [sem(f"b_stored{p}") for p in range(2)]

    NU = NSTRIP * UPS
    bank = {kind: bank - half for kind, half, _, bank in BLOCK_TURNS}
    turn = {(kind, half): n for n, (kind, half, _, _) in enumerate(BLOCK_TURNS)}
    qkv_t, proj_t, mlp_t = c["qkv_t"]["b"], c["proj_t"]["b"], c["mlp_t"]["b"]

    def over(eng, body):
        body(-1, -1, 1)
        body(0, 0, 0)
        pairs = (NSTRIP - 3) // 2
        with eng.Fori(0, pairs) as i:
            body(i * 2 + 1, i, 1)
            body(i * 2 + 2, i + 1, 0)
        for s in range(1 + 2 * pairs, NSTRIP + 1):
            body(s, s // 2, s % 2)

    with nc.Block() as block:
        @block.sync
        def _(sp):
            def load(s):
                if positive(s):
                    sp.wait_ge(normed, s)
                sp.dma_start(strip[:, :], x_flat[:, bass.ds(s * STRIP, STRIP)]).then_inc(x_in, 16)

            def body(s, sh, p):
                if there(s + 2, NSTRIP):
                    load(s + 2)
                for i in range(UPS):
                    half = i // 2
                    if there(s + 1, NSTRIP) and i % 2:
                        cols = slice(half * HS, (half + 1) * HS)
                        u = (s + 1) * UPS + i
                        sp.wait_ge(taken["q"], u + 1)
                        sp.wait_ge(taken["k"], u + 1)
                        for h in range(NH):
                            for n in range(4):
                                first, step = Q_COPIES[n], 2 + K_COPIES[n] - Q_COPIES[n]
                                sp.dma_start(stack[half][HD * n:HD * (n + 1), :, h, 0:HS],
                                             parts[HD * h:HD * (h + 1), first:first + step + 1:step, cols]
                                             ).then_inc(stacked[half], 16)
                    if i == 1 and there(s - 1, NSTRIP):
                        sp.wait_ge(unit_done, s * UPS)
                        sp.dma_start(net_flat[:, bass.ds((s - 1) * STRIP, STRIP)],
                                     done_strip[:, 1 - p, :]).then_inc(stored[1 - p], 16)

            load(0)
            over(sp, body)
            for p in range(2):
                sp.wait_ge(stored[p], 16 * (NSTRIP // 2))

        @block.tensor
        def _(t):
            def enter(kind, k_step, half=0):
                before = tenant_before(BLOCK_TURNS, BLOCK_PER, k_step, turn[kind, half], NU)
                if before:
                    t.wait_ge(taken[before[0]], before[1])

            def body(s, sh, p):
                for i in range(UPS):
                    u = s * UPS + i
                    b = i % 2
                    done, half = u - 2, i // 2
                    if there(u, NU):
                        t.wait_ge(stacked[half], RESTACK * (s + 1))
                        if positive(u - 1):
                            t.wait_ge(biased, u - 1)
                        for h in range(NH):
                            for n in range(WPU):
                                col = ((i % 2) * WPU + n) * BT
                                mm = t.matmul(s_ps[PAD * (n % 2):PAD * (n % 2 + 1), b, h, (n // 2) * BT:(n // 2 + 1) * BT],
                                              stack[half][:, 0, h, col:col + PAD], stack[half][:, 1, h, col:col + BT],
                                              start=True, stop=True)
                        mm.then_inc(scored, 1)
                    if there(done, NU):
                        t.wait_ge(taken["o"], u - 1)
                        enter("pj", u)
                        t.matmul(m_ps[:, bank["pj"], 0:UT], proj_t[:, :], att[:, b, :],
                                 start=True, stop=True).then_inc(made["pj"], 1)
                    if there(u - 1, NU):
                        t.wait_ge(probs_made, u)
                        for k in range(2):
                            enter("t", u, k)
                            for n in range(4):
                                blk = 4 * k + n
                                mm = t.transpose(m_ps[:, bank["t"] + k, n * P:(n + 1) * P],
                                                 probs[:, 1 - b, blk // 2, 2 * (blk % 2):2 * (blk % 2) + 2, :]
                                                 .rearrange("p h m -> p (h m)"),
                                                 c["ident"][:, :])
                            mm.then_inc(made["t"], 1)
                    if there(done, NU):
                        t.wait_ge(taken["pj"], u - 1)
                        enter("cz", u)
                        t.matmul(m_ps[:, bank["cz"], 0:UT], c["center"][:, :], z[:, b, :],
                                 start=True, stop=True).then_inc(made["cz"], 1)
                    if there(s + 1, NSTRIP):
                        if i == 0:
                            t.wait_ge(normed, s + 2)
                        enter("v", u)
                        for n in range(WPU):
                            col = (i * WPU + n) * BT
                            for odd in range(2):
                                wv = qkv_t[:, 2 * P:3 * P].rearrange("p (a o d) -> p a o d", a=2, o=2)[:, :, odd, :]
                                to = m_ps[PAD * odd:PAD * (odd + 1), bank["v"], n * 64:(n + 1) * 64]
                                mm = t.matmul(to.rearrange("p (a d) -> p a d", a=2),
                                              xn[:, 1 - p, col:col + PAD], wv, start=True, stop=True)
                        mm.then_inc(made["v"], 1)
                    if there(done, NU):
                        t.wait_ge(taken["cz"], u - 1)
                        enter("var", u)
                        t.matmul(m_ps[:, bank["var"], 0:UT], c["mean_w"][:, :], sq[:, :],
                                 start=True, stop=True).then_inc(made["var"], 1)
                    if there(u - 1, NU):
                        t.wait_ge(taken["t"], 2 * u)
                        q = (i - 1) % UPS
                        pv = p if i else 1 - p
                        t.wait_ge(taken["v"], u)
                        enter("o", u)
                        for n in range(WPU):
                            for a in range(2):
                                at = (n * 2 + a) * 64
                                mm = t.matmul(m_ps[64 * a:64 * (a + 1), bank["o"], n * BT:(n + 1) * BT],
                                              vals[:, pv, q, at:at + 64],
                                              probs_t[:, 1 - b, (n // 2) * 2 + a, PAD * (n % 2):PAD * (n % 2) + BT],
                                              start=True, stop=True)
                        mm.then_inc(made["o"], 1)
                    if there(done, NU):
                        enter("y", u)
                        t.matmul(m_ps[:, bank["y"], 0:UT], mlp_t[:, :], z[:, b, :],
                                 start=True, stop=True).then_inc(made["y"], 1)
                    if there(s + 1, NSTRIP):
                        enter("q", u)
                        t.matmul(m_ps[:, bank["q"], 0:UT], qkv_t[:, 0:P], xn[:, 1 - p, i * UT:(i + 1) * UT],
                                 start=True, stop=True).then_inc(made["q"], 1)
                    if there(s + 1, NSTRIP):
                        enter("k", u)
                        t.matmul(m_ps[:, bank["k"], 0:UT], qkv_t[:, P:2 * P], xn[:, 1 - p, i * UT:(i + 1) * UT],
                                 start=True, stop=True).then_inc(made["k"], 1)

            t.wait_ge(zeroed, 6)
            over(t, body)

        @block.scalar
        def _(a):
            def high(kind, slot, s, i, u):
                if positive(s + 1):
                    a.wait_ge(stacked[i // 2], RESTACK * (s + 1))
                a.wait_ge(made[kind], u + UPS + 1)
                a.activation(parts[:, slot, i * UT:(i + 1) * UT], m_ps[:, bank[kind], 0:UT],
                             ACT.Copy).then_inc(high_made[kind], 1)

            def body(s, sh, p):
                for i in range(UPS):
                    u = s * UPS + i
                    b = i % 2
                    if there(u - 1, NU):
                        for k in range(2):
                            a.wait_ge(made["t"], (u - 1) * 2 + k + 1)
                            if positive(u - 2):
                                a.wait_ge(made["o"], u - 2)
                            a.activation(probs_t[:, 1 - b, 4 * k:4 * k + 4, :], m_ps[:, bank["t"] + k, :],
                                         ACT.Copy).then_inc(taken["t"], 1)
                    if there(u - 2, NU):
                        a.wait_ge(made["cz"], u - 1)
                        if positive(u - 2):
                            a.wait_ge(made["var"], u - 2)
                        a.activation(sq[:, :], m_ps[:, bank["cz"], 0:UT], ACT.Square).then_inc(taken["cz"], 1)
                    if there(s + 1, NSTRIP):
                        a.wait_ge(made["v"], u + UPS + 1)
                        v5 = vals[:, 1 - p, i, :].rearrange("p (n o d) -> p n o d", o=2, d=HD)
                        m4 = m_ps[:, bank["v"], :].rearrange("p (n d) -> p n d", d=HD)
                        a.activation(v5[0:64, :, 0, :], m4[0:64], ACT.Copy)
                        a.activation(v5[64:128, :, 1, :], m4[64:128], ACT.Copy).then_inc(taken["v"], 1)
                    if there(u, NU):
                        a.wait_ge(shift_done, u + 1)
                        if positive(u - 1):
                            a.wait_ge(probs_made, u - 1)
                        a.activation(expd[:, :, :], shifted[:, :, :], ACT.Exp).then_inc(exp_done, 1)
                    if there(u - 2, NU):
                        a.wait_ge(made["var"], u - 1)
                        a.activation(lnv[:, :], m_ps[:, bank["var"], 0:UT], ACT.Ln,
                                     bias=c["eps"][:, 0:1]).then_inc(taken["var"], 1)
                        a.wait_ge(taken["var"], u - 1)
                        if positive(u - 2):
                            a.wait_ge(taken["y"], u - 2)
                        a.activation(rstd[:, :], lnv[:, :], ACT.Exp, scale=-0.5).then_inc(rstd_made, 1)
                    if there(u - 1, NU):
                        a.wait_ge(made["o"], u)
                        if positive(u - 2):
                            a.wait_ge(made["pj"], u - 2)
                        a.activation(att[:, 1 - b, :], m_ps[:, bank["o"], 0:UT], ACT.Copy).then_inc(taken["o"], 1)
                    if there(s + 1, NSTRIP):
                        high("q", 0, s, i, u)
                    if there(s + 1, NSTRIP):
                        high("k", 2, s, i, u)

            a.wait_ge(zeroed, 6)
            over(a, body)

        @block.vector
        def _(v):
            def norm_strip(s, p):
                v.wait_ge(x_in, (s + 1) * 16)
                if positive(s - 1):
                    v.wait_ge(made["k"], (s - 1) * UPS)
                    v.wait_ge(res_made, s - 1)
                v.tensor_scalar(xn[:, p, 0:STRIP].rearrange("p (w r c) -> p w r c", r=BW, c=BW),
                                strip[:, :].rearrange("p (r w c) -> p w r c", r=BW, c=BW),
                                c["gn_scale"][:, 0:1], c["gn_shift"][:, 0:1], ALU.mult, ALU.add).then_inc(normed, 1)

            def low(kind, slot, i, u):
                v.wait_ge(high_made[kind], u + UPS + 1)
                cols = slice(i * UT, (i + 1) * UT)
                v.tensor_tensor(parts[:, slot + 1, cols], m_ps[:, bank[kind], 0:UT], parts[:, slot, cols],
                                ALU.subtract).then_inc(taken[kind], 1)

            def body(s, sh, p):
                for i in range(UPS):
                    u = s * UPS + i
                    b = i % 2
                    if there(u - 2, NU):
                        v.wait_ge(made["pj"], u - 1)
                        if positive(u - 3):
                            v.wait_ge(made["y"], u - 3)
                        q = (i - 2) % UPS
                        pr = p if i >= 2 else 1 - p
                        if i >= 2:
                            v.wait_ge(res_made, s + 1)
                        v.tensor_tensor(z[:, b, :], m_ps[:, bank["pj"], 0:UT],
                                        res[:, pr, q * UT:(q + 1) * UT], ALU.add).then_inc(taken["pj"], 1)
                    if there(u, NU):
                        v.wait_ge(scored, u + 1)
                        v.tensor_tensor(score[:, :, :].rearrange("p (h n) m -> p h n m", h=NH),
                                        s_ps[:, b, :, 0:PPU * BT].rearrange("p h (n m) -> p h n m", m=BT),
                                        spread(c["bbias"][:, :, :], 2, PPU), ALU.add).then_inc(biased, 1)
                        v.wait_ge(biased, u + 1)
                        v.tensor_reduce(row_max[:, b, :], score[:, :, :], AX_X, ALU.max).then_inc(maxed, 1)
                        v.wait_ge(maxed, u + 1)
                        if positive(u - 1):
                            v.wait_ge(exp_done, u - 1)
                        v.tensor_tensor(shifted[:, :, :], score[:, :, :], spread(row_max[:, b, :], 2, BT),
                                        ALU.subtract).then_inc(shift_done, 1)
                    if there(u, NU):
                        v.wait_ge(exp_done, u + 1)
                        v.tensor_reduce(row_sum[:, b, :], expd[:, :, :], AX_X, ALU.add).then_inc(summed, 1)
                        v.wait_ge(summed, u + 1)
                        v.reciprocal(row_inv[:, b, :], row_sum[:, b, :]).then_inc(inverted, 1)
                        v.wait_ge(inverted, u + 1)
                        if positive(u - 1):
                            v.wait_ge(made["t"], 2 * (u - 1))
                        v.tensor_tensor(probs[:, b, :, :, 0:BT].rearrange("p n h m -> p h n m"),
                                        expd[:, :, :].rearrange("p (h n) m -> p h n m", h=NH),
                                        spread(row_inv[:, b, :].rearrange("p (h n) -> p h n", h=NH), 3, BT),
                                        ALU.mult).then_inc(probs_made, 1)
                    if there(s + 1, NSTRIP):
                        low("q", 0, i, u)
                    if there(u - 2, NU):
                        v.wait_ge(made["y"], u - 1)
                        v.wait_ge(rstd_made, u - 1)
                        if positive(u - 3):
                            v.wait_ge(unit_done, u - 3)
                        v.tensor_tensor(y[:, b, :], m_ps[:, bank["y"], 0:UT], rstd[:, :],
                                        ALU.mult).then_inc(taken["y"], 1)
                    if i == UPS - 1 and there(s + 2, NSTRIP):
                        norm_strip(s + 2, p)
                    if there(s + 1, NSTRIP):
                        low("k", 2, i, u)

            v.wait_ge(zeroed, 6)
            norm_strip(0, 0)
            over(v, body)

        @block.gpsimd
        def _(g):
            g.memset(probs[:, :, :, :, :], 0.0).then_inc(zeroed, 1)
            g.memset(vals[:, 0, :, :], 0.0).then_inc(zeroed, 1)
            g.memset(vals[:, 1, :, :], 0.0).then_inc(zeroed, 1)
            g.memset(xn[:, :, STRIP:WIDE], 0.0).then_inc(zeroed, 1)
            g.memset(stack[0][:, 0, :, HS:], 0.0).then_inc(zeroed, 1)
            g.memset(stack[1][:, 0, :, HS:], 0.0).then_inc(zeroed, 1)

            def body(s, sh, p):
                for i in range(UPS):
                    u = s * UPS + i
                    b = i % 2
                    if i == 2 and there(s + 1, NSTRIP):
                        g.wait_ge(normed, s + 2)
                        if positive(s):
                            g.wait_ge(taken["pj"], s * UPS)
                        g.nop(nofuse=True)
                        g.tensor_scalar(res[:, 1 - p, :], xn[:, 1 - p, 0:STRIP], c["proj_b"]["b"][:, 0:1], None,
                                        ALU.add).then_inc(res_made, 1)
                    if there(u - 2, NU):
                        q = (i - 2) % UPS
                        pd = p if i >= 2 else 1 - p
                        if i == 2 and positive(s - 1):
                            g.wait_ge(stored[p], 16 * sh)
                        g.wait_ge(taken["y"], u - 1)
                        dst = done_strip[:, pd, :].rearrange("p (r c w) -> p w r c", r=BW, c=BW)[:, q * WPU:(q + 1) * WPU]
                        g.nop(nofuse=True)
                        g.tensor_scalar(dst, y[:, b, :].rearrange("p (w r c) -> p w r c", r=BW, c=BW),
                                        c["out_b"]["b"][:, 0:1], None, ALU.add).then_inc(unit_done, 1)

            over(g, body)


def grid_stage(nc, own, net1, net2, c):
    def sb(name, shape, dt=F32):
        return own.enter_context(nc.sbuf_tensor(name, shape, dt))

    def sem(name):
        return own.enter_context(nc.semaphore(name))

    tokens = sb("tokens", [P, TPP, P])
    win = [sb(f"win{p}", [P, GT]) for p in range(2)]
    res = sb("g_res", [P, GT])
    qh, ql = sb("g_qh", [P, GT], F16), sb("g_ql", [P, GT], F16)
    kh, kl = sb("g_kh", [P, GT], F16), sb("g_kl", [P, GT], F16)
    qstack = [sb(f"g_qstack{p}", [P, NH, GT], F16) for p in range(2)]
    kstack = [sb(f"g_kstack{p}", [P, NH, GT], F16) for p in range(2)]
    vals = [sb(f"g_vals{p}", [P, QT, P]) for p in range(2)]
    score = sb("g_score", [P, 2, GT])
    probs = sb("g_probs", [P, 2, GT])
    probs_t = [sb(f"g_probs_t{g}", [P, NH, QT, QG * P]) for g in range(2)]
    row_min = sb("row_min", [P, 2])
    row_sum = sb("g_row_sum", [P, 2, UNITS])
    row_inv = sb("g_row_inv", [P, 2, UNITS // 2])
    inv_wide = sb("inv_wide", [P, QT // 2, P])
    att_raw = sb("att_raw", [P, HALF])
    att = sb("g_att", [P, HALF])
    z = sb("g_z", [P, HALF])
    sq = sb("g_sq", [P, HALF])
    lnv = sb("g_lnv", [P, HALF])
    rstd = sb("g_rstd", [P, HALF])
    y = sb("g_y", [P, HALF])
    fin = sb("fin", [P, 2, HALF])
    s_ps = own.enter_context(nc.psum_tensor("g_s_ps", [P, 2, GT], F32))
    t_ps = own.enter_context(nc.psum_tensor("g_t_ps", [P, 2, 512], F32))
    o_ps = own.enter_context(nc.psum_tensor("g_o_ps", [P, 512], F32))
    m_ps = own.enter_context(nc.psum_tensor("g_m_ps", [P, 512], F32))

    tokens_in = sem("g_tokens_in")
    stored = [sem(f"g_stored{h}") for h in range(2)]
    q_stacked, k_stacked = sem("g_q_stacked"), sem("g_k_stacked")
    high_made = {k: sem(f"g_{k}_high") for k in "qk"}
    scored = sem("g_scored")
    biased = sem("g_biased")
    exp_done = sem("g_exp_done")
    turned = sem("g_turned")
    pt_copied = [sem(f"g_pt_copied{k}") for k in range(2)]
    group_done = sem("g_group_done")
    att_copied = sem("g_att_copied")
    inverted = sem("g_inverted")
    widened = sem("g_widened")
    res_made = sem("g_res_made")
    rstd_made = sem("g_rstd_made")
    fin_done = sem("g_fin_done")
    made = {k: sem(f"g_pe_{k}") for k in KINDS}
    taken = {k: sem(f"g_took_{k}") for k in KINDS}

    qkv_t, proj_t, mlp_t = c["qkv_t"]["g"], c["proj_t"]["g"], c["mlp_t"]["g"]
    GPW = UNITS // GROUP

    def over(eng, body):
        body(-1, -1, 1)
        body(0, 0, 0)
        pairs = (NWIN - 3) // 2
        if pairs > 0:
            with eng.Fori(0, pairs) as i:
                body(i * 2 + 1, i, 1)
                body(i * 2 + 2, i + 1, 0)
        for w in range(1 + 2 * pairs, NWIN + 1):
            body(w, w // 2, w % 2)

    def turns_at(w, s):
        for n, (kind, half, off, _) in enumerate(GRID_TURNS):
            if TURN_STEPS[n] == s and there(w + off, NWIN):
                yield n, kind, half, w + off

    def count(v, half):
        return v * 2 + half + 1

    def value_step(w, s):
        n = s - LAG
        v = w if n >= 0 else w - 1
        n %= UNITS
        return (v, n // GROUP, n % GROUP) if there(v, NWIN) else None

    O_DONE = [LAG + UNITS // 2, LAG + UNITS - UNITS]

    net1_tokens = bass.AP(net1.tensor, 0, [[HW * P, HW], [TPP * P, HW // TPP], [1, TPP * P]])

    with nc.Block() as block:
        @block.sync
        def _(sp):
            def load(w):
                if positive(w):
                    sp.wait_ge(made["w"], 2 * w)
                src = net1_tokens[bass.ds((w // GN_) * GW, GW), bass.ds((w % GN_) * (GW // TPP), GW // TPP), :]
                sp.dma_start(tokens[:, :, :].rearrange("p t c -> p (t c)"), src).then_inc(tokens_in, 16)

            def store(w, half):
                sp.wait_ge(fin_done, count(w, half))
                dst = net2[:, bass.ds(w * GT + half * HALF, HALF)]
                sp.dma_start(dst, fin[:, half, :]).then_inc(stored[half], 16)

            def body(w, wh, p):
                if there(w - 1, NWIN):
                    store(w - 1, 0)
                if there(w + 1, NWIN):
                    sp.wait_ge(taken["k"], count(w + 1, 1))
                    restack(sp, kstack[1 - p], kh, kl, slice(0, GT), K_COPIES, k_stacked)
                if there(w - 1, NWIN):
                    store(w - 1, 1)
                if there(w + 1, NWIN):
                    sp.wait_ge(taken["q"], count(w + 1, 1))
                    restack(sp, qstack[1 - p], qh, ql, slice(0, GT), Q_COPIES, q_stacked)
                if there(w + 2, NWIN):
                    load(w + 2)

            load(0)
            over(sp, body)
            for half in range(2):
                sp.wait_ge(stored[half], 16 * NWIN)

        @block.tensor
        def _(t):
            def product(w, p, turn_at, kind, half, v):
                before = tenant_before(GRID_TURNS, GRID_PER, w, turn_at, NWIN)
                if before:
                    t.wait_ge(taken[before[0]], before[1])
                cols = slice(half * HALF, (half + 1) * HALF)
                if kind == "w":
                    t.wait_ge(tokens_in, 16 * (v + 1))
                    for n in range(TPP // 2):
                        mm = t.transpose(m_ps[:, n * P:(n + 1) * P], tokens[:, half * TPP // 2 + n, :], c["ident"][:, :])
                elif kind in ("k", "q"):
                    if kind == "k" and half == 0:
                        t.wait_ge(taken["w"], count(v, 1))
                    at = 0 if kind == "q" else P
                    mm = t.matmul(m_ps[:, :], qkv_t[:, at:at + P], win[1 - p][:, cols], start=True, stop=True)
                elif kind == "v":
                    for n in range(QT // 2):
                        at = half * HALF + n * P
                        mm = t.matmul(m_ps[:, n * P:(n + 1) * P], win[1 - p][:, at:at + P],
                                      qkv_t[:, 2 * P:3 * P], start=True, stop=True)
                elif kind == "r":
                    t.wait_ge(widened, count(v, half))
                    for n in range(QT // 2):
                        mm = t.transpose(m_ps[:, n * P:(n + 1) * P], inv_wide[:, n, :], c["ident"][:, :])
                elif kind == "pj":
                    t.wait_ge(taken["r"], count(v, half))
                    mm = t.matmul(m_ps[:, :], proj_t[:, :], att[:, :], start=True, stop=True)
                elif kind == "cz":
                    t.wait_ge(taken["pj"], count(v, half))
                    mm = t.matmul(m_ps[:, :], c["center"][:, :], z[:, :], start=True, stop=True)
                elif kind == "var":
                    t.wait_ge(taken["cz"], count(v, half))
                    mm = t.matmul(m_ps[:, :], c["mean_w"][:, :], sq[:, :], start=True, stop=True)
                else:
                    mm = t.matmul(m_ps[:, :], mlp_t[:, :], z[:, :], start=True, stop=True)
                mm.then_inc(made[kind], 1)

            def turn_half(w, u, k, b):
                n = w * UNITS + u
                if k == 0:
                    t.wait_ge(exp_done, n + 1)
                if positive(n):
                    t.wait_ge(pt_copied[k], n)
                for m in range(4):
                    at = (4 * k + m) * P
                    mm = t.transpose(t_ps[:, k, m * P:(m + 1) * P], probs[:, b, at:at + P], c["ident"][:, :])
                mm.then_inc(turned, 1)

            def body(w, wh, p):
                for s in range(UNITS):
                    b = s % 2
                    if there(w, NWIN):
                        if s == 0:
                            t.wait_ge(q_stacked, RESTACK * (w + 1))
                            t.wait_ge(k_stacked, RESTACK * (w + 1))
                        n = w * UNITS + s
                        if positive(n - 1):
                            t.wait_ge(biased, n - 1)
                        qt, h = s // NH, s % NH
                        for k in range(2):
                            mm = t.matmul(s_ps[:, b, k * 512:(k + 1) * 512], qstack[p][:, h, qt * P:(qt + 1) * P],
                                          kstack[p][:, h, k * 512:(k + 1) * 512], start=True, stop=True)
                        mm.then_inc(scored, 1)
                    v, u = (w, s - 2) if s >= 2 else (w - 1, s - 2 + UNITS)
                    for n, kind, half, at in turns_at(w, s):
                        product(w, p, n, kind, half, at)
                    if there(v, NWIN):
                        turn_half(v, u, 0, b)
                    if there(v, NWIN):
                        turn_half(v, u, 1, b)
                    step = value_step(w, s)
                    if step:
                        v, g, kt = step
                        pv = p if s >= LAG else 1 - p
                        col = (g % 2) * QG * P
                        if kt == 0:
                            last = v * UNITS + (g + 1) * GROUP
                            for k in range(2):
                                t.wait_ge(pt_copied[k], last)
                            if g == 0:
                                t.wait_ge(taken["v"], count(v, 1))
                            if g % 2 == 0 and positive(v * 2 + g // 2):
                                t.wait_ge(att_copied, v * 2 + g // 2)
                        for h in range(NH):
                            mm = t.matmul(o_ps[HD * h:HD * (h + 1), col:col + QG * P],
                                          vals[pv][:, kt, HD * h:HD * (h + 1)], probs_t[g % 2][:, h, kt, :],
                                          start=(kt == 0), stop=(kt == QT - 1))
                        if kt == QT - 1:
                            mm.then_inc(group_done, 1)

            over(t, body)

        @block.scalar
        def _(a):
            def read_bank(kind, half, v, p):
                if kind == "w":
                    a.wait_ge(made["w"], count(v, half))
                    if positive(v - 1):
                        a.wait_ge(res_made, v - 1)
                    dst = win[1 - p][:, :].rearrange("p (t j) -> p j t", j=TPP)
                    a.activation(dst[:, half * TPP // 2:(half + 1) * TPP // 2],
                                 m_ps[:, :].rearrange("p (j t) -> p j t", t=P), ACT.Copy).then_inc(taken["w"], 1)
                elif kind in ("k", "q"):
                    hi = kh if kind == "k" else qh
                    if half == 0 and positive(v):
                        a.wait_ge(k_stacked if kind == "k" else q_stacked, v * RESTACK)
                    a.wait_ge(made[kind], count(v, half))
                    a.activation(hi[:, half * HALF:(half + 1) * HALF], m_ps[:, :], ACT.Copy).then_inc(high_made[kind], 1)
                elif kind == "v":
                    a.wait_ge(made["v"], count(v, half))
                    if half == 0 and positive(v - 1):
                        a.wait_ge(group_done, (v - 1) * GPW)
                    n = QT // 2
                    a.activation(vals[1 - p][:, half * n:(half + 1) * n, :], m_ps[:, :], ACT.Copy).then_inc(taken["v"], 1)
                elif kind == "cz":
                    a.wait_ge(made["cz"], count(v, half))
                    if positive(count(v, half) - 1):
                        a.wait_ge(made["var"], count(v, half) - 1)
                    a.activation(sq[:, :], m_ps[:, :], ACT.Square).then_inc(taken["cz"], 1)
                elif kind == "var":
                    n = count(v, half)
                    a.wait_ge(made["var"], n)
                    a.activation(lnv[:, :], m_ps[:, :], ACT.Ln, bias=c["eps"][:, 0:1]).then_inc(taken["var"], 1)
                    a.wait_ge(taken["var"], n)
                    if positive(n - 1):
                        a.wait_ge(taken["y"], n - 1)
                    a.activation(rstd[:, :], lnv[:, :], ACT.Exp, scale=-0.5).then_inc(rstd_made, 1)

            def body(w, wh, p):
                for s in range(UNITS):
                    b = s % 2
                    for half in range(2):
                        if s == O_DONE[half]:
                            v = w - half
                            if there(v, NWIN):
                                n = count(v, half)
                                a.wait_ge(group_done, n * (GPW // 2))
                                if positive(n - 1):
                                    a.wait_ge(taken["r"], n - 1)
                                a.activation(att_raw[:, :], o_ps[:, :], ACT.Copy).then_inc(att_copied, 1)
                    for _, kind, half, at in turns_at(w, s):
                        read_bank(kind, half, at, p)
                    v, u = (w, s - 2) if s >= 2 else (w - 1, s - 2 + UNITS)
                    if there(v, NWIN):
                        n = v * UNITS + u
                        a.wait_ge(turned, 2 * n + 1)
                        g, qi, h = u // GROUP, (u // NH) % QG, u % NH
                        if u % GROUP == 0:
                            if positive(v * GPW + g - 1):
                                a.wait_ge(group_done, v * GPW + g - 1)
                        a.activation(probs_t[g % 2][:, h, 0:4, qi * P:(qi + 1) * P], t_ps[:, 0, :],
                                     ACT.Copy).then_inc(pt_copied[0], 1)
                    if there(w, NWIN):
                        n = w * UNITS + s
                        a.wait_ge(biased, n + 1)
                        if positive(n - 1):
                            a.wait_ge(turned, 2 * (n - 1))
                        if s == 0 and positive(w - 1):
                            a.wait_ge(inverted, 2 * (w - 1))
                        a.activation(probs[:, b, :], score[:, b, :], ACT.Exp, bias=row_min[:, b:b + 1], scale=-1.0,
                                     accum_out=row_sum[:, p, s:s + 1]).then_inc(exp_done, 1)

            over(a, body)

        @block.vector
        def _(v_):
            def read_bank(kind, half, v, p):
                n = count(v, half)
                if kind in ("k", "q"):
                    hi, lo = (kh, kl) if kind == "k" else (qh, ql)
                    cols = slice(half * HALF, (half + 1) * HALF)
                    v_.wait_ge(high_made[kind], n)
                    v_.tensor_tensor(lo[:, cols], m_ps[:, :], hi[:, cols], ALU.subtract).then_inc(taken[kind], 1)
                elif kind == "r":
                    v_.wait_ge(made["r"], n)
                    v_.wait_ge(att_copied, n)
                    if positive(n - 1):
                        v_.wait_ge(made["pj"], n - 1)
                    v_.tensor_tensor(att[:, :], m_ps[:, :], att_raw[:, :], ALU.mult).then_inc(taken["r"], 1)
                elif kind == "pj":
                    v_.wait_ge(made["pj"], n)
                    v_.wait_ge(res_made, v + 1)
                    if positive(n - 1):
                        v_.wait_ge(made["y"], n - 1)
                    v_.tensor_tensor(z[:, :], m_ps[:, :], res[:, half * HALF:(half + 1) * HALF],
                                     ALU.add).then_inc(taken["pj"], 1)
                elif kind == "y":
                    v_.wait_ge(made["y"], n)
                    v_.wait_ge(rstd_made, n)
                    if positive(n - 1):
                        v_.wait_ge(fin_done, n - 1)
                    v_.tensor_tensor(y[:, :], m_ps[:, :], rstd[:, :], ALU.mult).then_inc(taken["y"], 1)

            def body(w, wh, p):
                for s in range(UNITS):
                    b = s % 2
                    if there(w, NWIN):
                        n = w * UNITS + s
                        qt, h = s // NH, s % NH
                        v_.wait_ge(scored, n + 1)
                        if positive(n - 1):
                            v_.wait_ge(exp_done, n - 1)
                        v_.nop(nofuse=True)
                        at = (QT - 1 - qt) * RPT
                        v_.tensor_tensor_reduce(score[:, b, :], s_ps[:, b, :],
                                                c["gbias"][:, h, at:at + GW, :].rearrange("p r c -> p (r c)"),
                                                1.0, 3.0e38, ALU.add, ALU.min, row_min[:, b:b + 1]).then_inc(biased, 1)
                    for _, kind, half, at in turns_at(w, s):
                        read_bank(kind, half, at, p)
                    v, u = (w, s - 2) if s >= 2 else (w - 1, s - 2 + UNITS)
                    if there(v, NWIN):
                        n = v * UNITS + u
                        g, qi, h = u // GROUP, (u // NH) % QG, u % NH
                        v_.wait_ge(turned, 2 * n + 2)
                        if u % GROUP == 0 and positive(v * GPW + g - 1):
                            v_.wait_ge(group_done, v * GPW + g - 1)
                        v_.tensor_copy(probs_t[g % 2][:, h, 4:8, qi * P:(qi + 1) * P],
                                       t_ps[:, 1, :].rearrange("p (k q) -> p k q", k=4)).then_inc(pt_copied[1], 1)
                    for half in range(2):
                        if s == (UNITS // 2 + 2, 2)[half] and there(w - half, NWIN):
                            v = w - half
                            pr = 1 - p if half else p
                            v_.wait_ge(exp_done, v * UNITS + (half + 1) * UNITS // 2)
                            if positive(v):
                                v_.wait_ge(widened, 2 * v + half - 1)
                            v_.reciprocal(row_inv[:, half, :],
                                          row_sum[:, pr, half * UNITS // 2:(half + 1) * UNITS // 2]).then_inc(inverted, 1)

            over(v_, body)

        @block.gpsimd
        def _(g):
            def widen(v, half):
                n = count(v, half)
                g.wait_ge(inverted, n)
                if positive(n - 1):
                    g.wait_ge(made["r"], n - 1)
                g.nop(nofuse=True)
                inv = row_inv[:, half, :].rearrange("p (q h) -> p q h", h=NH)
                g.tensor_scalar(inv_wide[:, :, :].rearrange("p q (h d) -> p q h d", h=NH), spread(inv, 3, HD),
                                1.0, None, ALU.mult).then_inc(widened, 1)

            def finish(v, half):
                n = count(v, half)
                if positive(v):
                    g.wait_ge(stored[half], 16 * v)
                g.wait_ge(taken["y"], n)
                g.nop(nofuse=True)
                g.tensor_scalar(fin[:, half, :], y[:, :], c["out_b"]["g"][:, 0:1], None, ALU.add).then_inc(fin_done, 1)

            def body(w, wh, p):
                if there(w - 1, NWIN):
                    widen(w - 1, 1)
                    finish(w - 1, 0)
                if there(w, NWIN):
                    g.wait_ge(taken["w"], count(w, 1))
                    if positive(w):
                        g.wait_ge(taken["pj"], 2 * w)
                    g.nop(nofuse=True)
                    g.tensor_scalar(res[:, :], win[p][:, :], c["proj_b"]["g"][:, 0:1], None,
                                    ALU.add).then_inc(res_made, 1)
                if there(w - 1, NWIN):
                    finish(w - 1, 1)
                if there(w, NWIN):
                    widen(w, 0)

            over(g, body)


def last_stage(nc, own, x_flat, net2, out_flat, c):
    def sb(name, shape, dt=F32):
        return own.enter_context(nc.sbuf_tensor(name, shape, dt))

    def sem(name):
        return own.enter_context(nc.semaphore(name))

    ROW = GN_ * GT
    PIX = ROW // P
    TILES = GN_
    PIECES = GT // P
    rows = [sb(f"rows{p}", [P, GN_, GT]) for p in range(2)]
    mixed = sb("mixed", [P, 2, P, GN_])
    img = [sb(f"img{p}", [P, P, PIX]) for p in range(2)]
    t_ps = own.enter_context(nc.psum_tensor("l_t_ps", [P, 4, 2, 512], F32))

    rows_in = [sem(f"l_rows_in{p}") for p in range(2)]
    img_in = [sem(f"l_img_in{p}") for p in range(2)]
    stored = [sem(f"l_stored{p}") for p in range(2)]
    mix_done = sem("l_mixed")
    turned = sem("l_turned")
    added = sem("l_added")
    net2_rows = bass.AP(net2.tensor, 0, [[ROW, P * GN_], [1, ROW]])

    def over(eng, body):
        body(0, 0, 0)
        with eng.Fori(0, (TILES - 1) // 2) as i:
            body(i * 2 + 1, i, 1)
            body(i * 2 + 2, i + 1, 0)

    with nc.Block() as block:
        @block.sync
        def _(sp):
            def load(t, th, p):
                if positive(t - 1):
                    sp.wait_ge(mix_done, (t - 1) * PIECES)
                sp.dma_start(rows[p][:, :, :].rearrange("p w m -> p (w m)"),
                             net2_rows[bass.ds(t * P, P), :]).then_inc(rows_in[p], 16)

            over(sp, load)

        @block.gpsimd
        def _(g):
            def load(t, th, p):
                if positive(t - 1):
                    g.wait_ge(stored[p], 16 * th)
                g.dma_start(img[p][:, :, :].rearrange("p r t -> p (r t)"),
                            x_flat[:, bass.ds(t * P * PIX, P * PIX)]).then_inc(img_in[p], 16)

            over(g, load)

        @block.scalar
        def _(a):
            def body(t, th, p):
                a.wait_ge(rows_in[p], 16 * (th + 1))
                for k in range(PIECES):
                    n = t * PIECES + k
                    if positive(n - 1):
                        a.wait_ge(turned, n - 1)
                    a.activation(mixed[:, k % 2, :, :].rearrange("p m w -> p w m"),
                                 rows[p][:, :, k * P:(k + 1) * P], ACT.Copy).then_inc(mix_done, 1)
                a.wait_ge(added, (t + 1) * PIECES)
                a.dma_start(out_flat[:, bass.ds(t * P * PIX, P * PIX)],
                            img[p][:, :, :].rearrange("p r t -> p (r t)")).then_inc(stored[p], 16)

            over(a, body)
            a.wait_ge(stored[0], 16 * ((TILES + 1) // 2))
            a.wait_ge(stored[1], 16 * (TILES // 2))

        @block.tensor
        def _(t_):
            def body(t, th, p):
                for k in range(PIECES):
                    n = t * PIECES + k
                    t_.wait_ge(mix_done, n + 1)
                    if positive(n - 3):
                        t_.wait_ge(added, n - 3)
                    flat = mixed[:, k % 2, :, :].rearrange("p m w -> p (m w)")
                    for j in range(GN_):
                        at = (j % 4) * P
                        mm = t_.transpose(t_ps[:, k % 4, j // 4, at:at + P], flat[:, j * P:(j + 1) * P], c["ident"][:, :])
                    mm.then_inc(turned, 1)

            over(t_, body)

        @block.vector
        def _(v):
            def body(t, th, p):
                v.wait_ge(img_in[p], 16 * (th + 1))
                for k in range(PIECES):
                    v.wait_ge(turned, t * PIECES + k + 1)
                    to = img[p][:, :, k * GN_:(k + 1) * GN_]
                    src = t_ps[:, k % 4, :, :].rearrange("p b (t r) -> p r (b t)", r=P)[:, :, 0:GN_]
                    v.tensor_tensor(to, src, to, ALU.add).then_inc(added, 1)

            over(v, body)


_INS = [("x", (1, P, HW, HW))] + [
    (f"{p}_{name}", shape) for p, rel in (("b", BREL), ("g", GREL)) for name, shape in (
        ("table", (NH, rel, rel)), ("qkv_t", (P, 3 * P)), ("proj_t", (P, P)), ("proj_b", (P, 1)),
        ("ln_g", (P, 1)), ("ln_b", (P, 1)), ("fc1_w", (E, P)), ("fc1_b", (P, ET)),
        ("fc2_t", (E, P)), ("fc2_b", (P, 1)))]


def lay_out(inputs):
    arrays = {"x": np.ascontiguousarray(inputs["x"])}
    for p, rel in (("b", BREL), ("g", GREL)):
        def of(name, p=p):
            return np.asarray(inputs[f"L0_conv_{p}_{name}"])

        arrays[p + "_table"] = np.ascontiguousarray(of("rel_table").T.reshape(NH, rel, rel)[:, ::-1, ::-1])
        arrays[p + "_qkv_t"] = np.ascontiguousarray(of("qkv_w").T)
        arrays[p + "_proj_t"] = np.ascontiguousarray(of("proj_w").T)
        arrays[p + "_fc1_w"] = np.ascontiguousarray(of("fc1_w"))
        arrays[p + "_fc2_t"] = np.ascontiguousarray(of("fc2_w").T)
        arrays[p + "_fc1_b"] = np.ascontiguousarray(of("fc1_b").reshape(ET, P).T)
        for name in ("proj_b", "ln_g", "ln_b", "fc2_b"):
            arrays[f"{p}_{name}"] = np.ascontiguousarray(of(name).reshape(-1, 1))
    return arrays


def kernel(**inputs):
    import concourse.bacc as bacc
    from concourse.bass_utils import run_bass_kernel_spmd

    nc = bacc.Bacc("TRN2", target_bir_lowering=False, num_devices=1)
    arrays = lay_out(inputs)
    aps = {name: nc.dram_tensor(f"in_{name}", shape, F32, kind="ExternalInput").ap() for name, shape in _INS}
    out = nc.dram_tensor("out_0", (1, P, HW, HW), F32, kind="ExternalOutput").ap()
    net1 = nc.dram_tensor("net1", (P, HW, HW), F32, kind="Internal").ap()
    net2 = nc.dram_tensor("net2", (P, HW * HW), F32, kind="Internal").ap()
    build(nc, aps["x"], aps, out, net1, net2)
    done = run_bass_kernel_spmd(nc, [{f"in_{name}": arrays[name] for name, _ in _INS}], core_ids=[0])
    return done.results[0]["out_0"]
```
